# Optimizing a Trainium2 kernel written in Bass

```python
import numpy as np
import jax
import jax.numpy as jnp

def _softmax(x, axis=-1):
    return jax.nn.softmax(x, axis=axis)

def _gelu(x):
    return jax.nn.gelu(x, approximate=True)

def _silu(x):
    return jax.nn.silu(x)

def _sigmoid(x):
    return jax.nn.sigmoid(x)

def _layernorm(x, axis=-1, eps=1e-05):
    m = jnp.mean(x, axis=axis, keepdims=True)
    v = jnp.var(x, axis=axis, keepdims=True)
    return (x - m) / jnp.sqrt(v + eps)

def _scatter_add(tgt, idx, src, axis=0):
    return tgt.at[idx].add(src)

def _segment_sum(src, seg, n):
    return jax.ops.segment_sum(src, seg, n)
kernel_name = 'mk_seq_postln_d1_jaxref_r8_1ccf8b'

def setup_inputs(seed: int=0):
    np.random.seed(seed)
    _w = jnp.asarray

    def _L0_attn_setup():
        import jax, jax.numpy as jnp
        import numpy as np
        D_MODEL = 512
        N_Q = 32
        N_KV = 8
        HD = 128
        SLIDE = 64

        def _gqa_swa_attention(q, k, v, slide):
            B, Hq, N, D = q.shape
            Hkv = k.shape[1]
            G = Hq // Hkv
            qg = q.reshape(B, Hkv, G, N, D)
            scale = 1.0 / jnp.sqrt(jnp.asarray(D, q.dtype))
            s = jnp.einsum('bhgnd,bhmd->bhgnm', qg, k) * scale
            i = jnp.arange(N)[:, None]
            j = jnp.arange(N)[None, :]
            mask = j <= i
            if slide > 0:
                mask = mask & (i - j < slide)
            s = jnp.where(mask[None, None, None], s, jnp.asarray(-jnp.inf, s.dtype))
            p = jax.nn.softmax(s, axis=-1)
            o = jnp.einsum('bhgnm,bhmd->bhgnd', p, v)
            return o.reshape(B, Hq, N, D)
        key = jax.random.key(seed)
        ks = jax.random.split(key, 5)
        std = 0.01
        x = jax.random.normal(ks[0], (2, 256, D_MODEL), dtype=jnp.float32)
        wq = jax.random.normal(ks[1], (N_Q * HD, D_MODEL), dtype=jnp.float32) * std
        wk = jax.random.normal(ks[2], (N_KV * HD, D_MODEL), dtype=jnp.float32) * std
        wv = jax.random.normal(ks[3], (N_KV * HD, D_MODEL), dtype=jnp.float32) * std
        wo = jax.random.normal(ks[4], (D_MODEL, N_Q * HD), dtype=jnp.float32) * std
        return {'x': x, 'wq': wq, 'wk': wk, 'wv': wv, 'wo': wo}
    _L0_attn_in = _L0_attn_setup()

    def _L0_ffn_setup():
        import jax, jax.numpy as jnp
        import numpy as np
        BLOCK = 64
        NF4_CODE = jnp.array([-1.0, -0.6961928009986877, -0.5250730514526367, -0.39491748809814453, -0.28444138169288635, -0.18477343022823334, -0.09105003625154495, 0.0, 0.07958029955625534, 0.16093020141124725, 0.24611230194568634, 0.33791524171829224, 0.44070982933044434, 0.5626170039176941, 0.7229568362236023, 1.0], dtype=jnp.float32)

        def dequant_nf4(q, absmax, shape):
            w = NF4_CODE[q.reshape(-1)]
            w = w.reshape(-1, BLOCK) * absmax[:, None]
            return w.reshape(shape)
        key = jax.random.key(seed)
        ks = jax.random.split(key, 7)
        HD, M = (512, 1792)
        nblk = HD * M // BLOCK
        x = jax.random.normal(ks[0], (2, 256, HD), dtype=jnp.float32)
        gate_q = jax.random.randint(ks[1], (M, HD), 0, 16, dtype=jnp.int32)
        up_q = jax.random.randint(ks[2], (M, HD), 0, 16, dtype=jnp.int32)
        down_q = jax.random.randint(ks[3], (HD, M), 0, 16, dtype=jnp.int32)
        gate_absmax = jax.random.uniform(ks[4], (nblk,), dtype=jnp.float32) * 0.05
        up_absmax = jax.random.uniform(ks[5], (nblk,), dtype=jnp.float32) * 0.05
        down_absmax = jax.random.uniform(ks[6], (nblk,), dtype=jnp.float32) * 0.05
        return {'x': x, 'gate_q': gate_q, 'gate_absmax': gate_absmax, 'up_q': up_q, 'up_absmax': up_absmax, 'down_q': down_q, 'down_absmax': down_absmax}
    _L0_ffn_in = _L0_ffn_setup()
    _d = {'L0_attn_x': _L0_attn_in['x'], 'L0_attn_wq': _L0_attn_in['wq'], 'L0_attn_wk': _L0_attn_in['wk'], 'L0_attn_wv': _L0_attn_in['wv'], 'L0_attn_wo': _L0_attn_in['wo'], 'L0_ffn_gate_q': _L0_ffn_in['gate_q'], 'L0_ffn_gate_absmax': _L0_ffn_in['gate_absmax'], 'L0_ffn_up_q': _L0_ffn_in['up_q'], 'L0_ffn_up_absmax': _L0_ffn_in['up_absmax'], 'L0_ffn_down_q': _L0_ffn_in['down_q'], 'L0_ffn_down_absmax': _L0_ffn_in['down_absmax']}
    _x0 = _d['L0_attn_x']
    _d['L0_attn_x'] = jax.random.normal(jax.random.fold_in(jax.random.key(seed), 1), (8, 256, 512), dtype=_x0.dtype)
    del _x0
    return _d

def reference(L0_attn_x, L0_attn_wq, L0_attn_wk, L0_attn_wv, L0_attn_wo, L0_ffn_gate_q, L0_ffn_gate_absmax, L0_ffn_up_q, L0_ffn_up_absmax, L0_ffn_down_q, L0_ffn_down_absmax):

    def _L0_attn_ref(x, wq, wk, wv, wo):
        import jax, jax.numpy as jnp
        import numpy as np
        D_MODEL = 512
        N_Q = 32
        N_KV = 8
        HD = 128
        SLIDE = 64

        def _gqa_swa_attention(q, k, v, slide):
            B, Hq, N, D = q.shape
            Hkv = k.shape[1]
            G = Hq // Hkv
            qg = q.reshape(B, Hkv, G, N, D)
            scale = 1.0 / jnp.sqrt(jnp.asarray(D, q.dtype))
            s = jnp.einsum('bhgnd,bhmd->bhgnm', qg, k) * scale
            i = jnp.arange(N)[:, None]
            j = jnp.arange(N)[None, :]
            mask = j <= i
            if slide > 0:
                mask = mask & (i - j < slide)
            s = jnp.where(mask[None, None, None], s, jnp.asarray(-jnp.inf, s.dtype))
            p = jax.nn.softmax(s, axis=-1)
            o = jnp.einsum('bhgnm,bhmd->bhgnd', p, v)
            return o.reshape(B, Hq, N, D)
        B, N, _ = x.shape
        q = (x @ wq.T).reshape(B, N, N_Q, HD).transpose(0, 2, 1, 3)
        k = (x @ wk.T).reshape(B, N, N_KV, HD).transpose(0, 2, 1, 3)
        v = (x @ wv.T).reshape(B, N, N_KV, HD).transpose(0, 2, 1, 3)
        o = _gqa_swa_attention(q, k, v, SLIDE)
        o = o.transpose(0, 2, 1, 3).reshape(B, N, N_Q * HD)
        return o @ wo.T

    def _L0_ffn_ref(x, gate_q, gate_absmax, up_q, up_absmax, down_q, down_absmax):
        import jax, jax.numpy as jnp
        import numpy as np
        BLOCK = 64
        NF4_CODE = jnp.array([-1.0, -0.6961928009986877, -0.5250730514526367, -0.39491748809814453, -0.28444138169288635, -0.18477343022823334, -0.09105003625154495, 0.0, 0.07958029955625534, 0.16093020141124725, 0.24611230194568634, 0.33791524171829224, 0.44070982933044434, 0.5626170039176941, 0.7229568362236023, 1.0], dtype=jnp.float32)

        def dequant_nf4(q, absmax, shape):
            w = NF4_CODE[q.reshape(-1)]
            w = w.reshape(-1, BLOCK) * absmax[:, None]
            return w.reshape(shape)
        HD = x.shape[-1]
        M = gate_q.shape[0]
        Wg = dequant_nf4(gate_q, gate_absmax, (M, HD))
        Wu = dequant_nf4(up_q, up_absmax, (M, HD))
        Wd = dequant_nf4(down_q, down_absmax, (HD, M))
        g = jnp.einsum('bsh,mh->bsm', x, Wg)
        u = jnp.einsum('bsh,mh->bsm', x, Wu)
        h = jax.nn.silu(g) * u
        return jnp.einsum('bsm,hm->bsh', h, Wd)
    x = L0_attn_x
    x = _layernorm(x + _L0_attn_ref(x, L0_attn_wq, L0_attn_wk, L0_attn_wv, L0_attn_wo), axis=-1)
    x = _layernorm(x + _L0_ffn_ref(x, L0_ffn_gate_q, L0_ffn_gate_absmax, L0_ffn_up_q, L0_ffn_up_absmax, L0_ffn_down_q, L0_ffn_down_absmax), axis=-1)
    return x

_drawn_inputs = setup_inputs


def setup_inputs(seed=0):
    import zlib

    import numpy as np

    out = dict(_drawn_inputs(seed))
    spreads = {}
    factors = {'L0_attn_wq': 8.0,
     'L0_attn_wk': 8.0,
     'L0_ffn_gate_absmax': 3.011,
     'L0_ffn_up_absmax': 3.035,
     'L0_ffn_down_absmax': 3.033}
    for name, (base, spread) in spreads.items():
        noise = np.random.default_rng([zlib.crc32(name.encode()), seed]).standard_normal(out[name].shape)
        drawn = base * np.exp(spread * noise) if base else spread * noise
        out[name] = jnp.asarray(drawn.astype(out[name].dtype))
    for name, factor in factors.items():
        out[name] = (out[name] * factor).astype(out[name].dtype)
    return out
```

```python
from contextlib import ExitStack

import numpy as np

import concourse.bass as bass
from concourse import mybir

F32 = mybir.dt.float32
F32R = mybir.dt.float32r
ALU = mybir.AluOpType
ACT = mybir.ActivationFunctionType
AX_X = mybir.AxisListType.X

P = 128
NF4_CODE = [-1.0, -0.6961928009986877, -0.5250730514526367, -0.39491748809814453,
            -0.28444138169288635, -0.18477343022823334, -0.09105003625154495, 0.0,
            0.07958029955625534, 0.16093020141124725, 0.24611230194568634, 0.33791524171829224,
            0.44070982933044434, 0.5626170039176941, 0.7229568362236023, 1.0]


def code_lines():
    lines = []
    for k in range(0, len(NF4_CODE), 2):
        base, top = np.float32(NF4_CODE[k]), np.float32(NF4_CODE[k + 1])
        slope = np.float32(top - base)
        for s in (slope, np.nextafter(slope, np.float32(9)), np.nextafter(slope, np.float32(-9))):
            if np.float32(base + s) == top:
                lines.append((float(base), float(s)))
                break
    assert len(lines) == len(NF4_CODE) // 2
    return lines


MASKED = -3.0e38
LN_EPS = 1e-5
HI, LO = 0, 1
PASSES = ((HI, HI), (HI, LO), (LO, HI))


def decoder_layer(nc, x, xT, w_qkv, w_o, codes, absmax, masks, identity, out):
    _, KT, T = xT.shape
    G, _, _ = w_qkv.shape
    D = KT * P
    N = 256
    B = T // N
    HQ = 4
    QB = 64
    NB = N // QB
    GC = 6 * 512
    CHUNKS, _, CW = codes.shape
    MG = CHUNKS * CW // GC
    TB = T // 512
    TT = T // P
    SCALE = float(P) ** -0.5
    WINDOW_START = (0, 0, QB, 2 * QB)
    WINDOW = (0, 0, 1, 2)
    assert N == 256 and HQ == 4 and NB == 4 and CHUNKS == G * B and MG % 2 == 1 and T % 512 == 0

    ctx = ExitStack()
    with ctx:
        def sb(name, shape, dt=F32):
            return ctx.enter_context(nc.sbuf_tensor(name, shape, dt))

        def sem(name):
            return ctx.enter_context(nc.semaphore(name))

        parked = nc.dram_tensor("ffn_parts", [P, 2, MG * GC], F32, kind="Internal").ap()

        x_parts = sb("x_parts", [P, 2, KT, T], F32R)
        acc = sb("acc", [P, TT, D])
        x_raw = acc[:, :, :].rearrange("p t d -> p (t d)").rearrange("p (k t) -> p k t", k=KT)
        UW = KT * 256
        sizes = [2 * 3 * UW, 2 * HQ * D, 2 * HQ * N, 2 * N, 2 * 3 * P, 2 * HQ * N, 2 * HQ * N]
        rounded = sb("rounded", [P, sum(sizes)], F32R)
        at = [sum(sizes[:n]) for n in range(len(sizes))]

        def part(n):
            return rounded[:, at[n]:at[n] + sizes[n]]

        w_parts = part(0).rearrange("p (s u k c) -> p s u k c", s=2, u=3, k=KT)
        wo_parts = part(1).rearrange("p (s h d) -> p s h d", s=2, h=HQ)
        q_parts = part(2).rearrange("p (s c j m) -> p s c j m", s=2, c=2, j=NB)
        k_parts = part(3).rearrange("p (s t) -> p s t", s=2)
        v_parts = part(4).rearrange("p (s w d) -> p s w d", s=2, w=3)
        pt_parts = part(5).rearrange("p (s b m) -> p s b m", s=2, b=2)
        o_parts = part(6).rearrange("p (s h t) -> p s h t", s=2, h=HQ)
        ffn_w = [rounded[:, n * 2 * GC:(n + 1) * 2 * GC].rearrange("p (s i c) -> p s i c", s=2, i=6)
                 for n in range(2)]
        hid = [rounded[:, 4 * GC + n * 2048:4 * GC + (n + 1) * 2048]
               .rearrange("p (s c t) -> p s c t", s=2, c=2) for n in range(2)]
        raw = sb("raw", [P, 3 * UW + HQ * D])
        w_raw = raw[:, 0:3 * UW].rearrange("p (u n) -> p u n", u=3)
        wo_raw = raw[:, 3 * UW:3 * UW + HQ * D]
        silu_g = raw[:, 0:1024].rearrange("p (c t) -> p c t", c=2)
        hid_f = raw[:, 1024:2048].rearrange("p (c t) -> p c t", c=2)
        vT = sb("vT", [P, N])
        probs = sb("probs", [P, 2, NB * P])
        mask_sb = sb("mask_sb", [P, 2, P])
        ident = sb("ident", [P, P])
        row_max = sb("row_max", [P, 2, NB])
        neg_max = sb("neg_max", [P, 2, NB])
        row_sum = sb("row_sum", [P, 2, NB])
        row_inv = sb("row_inv", [P, 2, NB])
        stats = sb("stats", [P, TT, 6])
        mean_var = sb("mean_var", [P, TT, 2])
        rstd = sb("rstd", [P, TT])
        eps_sb = sb("eps_sb", [P, 1])
        code_sb = sb("code_sb", [P, CW], mybir.dt.int32)
        code_bits = sb("code_bits", [P, 4, CW], mybir.dt.uint8)
        absmax_sb = sb("absmax_sb", [P, CW])
        pair_value = sb("pair_value", [P, 8, CW])
        w_value, w_scaled, w_split = pair_value[:, 0, :], pair_value[:, 1, :], pair_value[:, 2:4, :]

        bank = [ctx.enter_context(nc.psum_tensor(f"bank{n}", [P, 512], F32)) for n in range(8)]
        PROJ, SCORE, TURN, CTX = bank[0:2], bank[2:4], bank[4:6], bank[6:8]

        x_loaded = [sem(f"x_loaded{n}") for n in range(2)]
        acc_loaded = sem("acc_loaded")
        consts_loaded = sem("consts_loaded")
        w_loaded, wo_loaded = sem("w_loaded"), sem("wo_loaded")
        codes_loaded, absmax_loaded = sem("codes_loaded"), sem("absmax_loaded")
        parked_sem = sem("parked")
        ffn_loaded = [sem("ffn_loaded0"), sem("ffn_loaded1")]
        out_stored = sem("out_stored")
        probs_ready, scaled, absmax_used, w_split_ready = (
            sem("probs_ready"), sem("scaled"), sem("absmax_used"), sem("w_split_ready"))
        q_done, kv_done, v_turned = sem("q_done"), sem("kv_done"), sem("v_turned")
        scores_done, probs_turned = sem("scores_done"), sem("probs_turned")
        ctx_done, y_done = sem("ctx_done"), sem("y_done")
        x1_turned, gu_done, down_done = sem("x1_turned"), sem("gu_done"), sem("down_done")
        x_hi, w_hi, wo_hi = sem("x_hi"), sem("w_hi"), sem("wo_hi")
        q_hi, k_hi, v_hi, vT_copied = sem("q_hi"), sem("k_hi"), sem("v_hi"), sem("vT_copied")
        exp_done, pt_hi, o_hi = sem("exp_done"), sem("pt_hi"), sem("o_hi")
        std_done, x1_hi = sem("std_done"), sem("x1_hi")
        pairs_ready = sem("pairs_ready")
        silu_done, hid_hi = sem("silu_done"), sem("hid_hi")
        x_lo, w_lo, wo_lo = sem("x_lo"), sem("w_lo"), sem("wo_lo")
        q_lo, k_lo, v_lo = sem("q_lo"), sem("k_lo"), sem("v_lo")
        max_found, neg_max_ready, inv_ready = sem("max_found"), sem("neg_max_ready"), sem("inv_ready")
        bits_ready, merged = sem("bits_ready"), sem("merged")
        pt_lo, o_lo, y_added = sem("pt_lo"), sem("o_lo"), sem("y_added")
        eps_set, stats_done, var_done, rstd_done, x1_normed, x1_lo = (
            sem("eps_set"), sem("stats_done"), sem("var_done"), sem("rstd_done"), sem("x1_normed"),
            sem("x1_lo"))
        hid_ready, hid_lo, out_normed = sem("hid_ready"), sem("hid_lo"), sem("out_normed")

        def f32(ap):
            return ap.bitcast(F32)

        def attention_steps(eng, step, at_group=None):
            with eng.Fori(0, G - 1) as g:
                if at_group is not None:
                    at_group(g)
                with eng.Fori(1, B) as b:
                    step(g * B + b, b, g * B + b - 1, b - 1, g, None)
                step(g * B + B, 0, g * B + B - 1, B - 1, g, g + 1)
            with eng.Fori(1, B) as b:
                step((G - 1) * B + b, b, (G - 1) * B + b - 1, b - 1, G - 1, None)
            step(None, None, G * B - 1, B - 1, G - 1, None)

        def ffn_steps(eng, step):
            def ids(pair, n):
                mg = n // TB
                return pair * (2 * TB) + n, pair * 2 + mg, pair + mg // 2, n % TB, mg % 2, n % 2

            step(ids(0, 0), None)
            with eng.Fori(0, MG // 2) as pair:
                for n in range(2 * TB):
                    step(ids(pair, n + 1), ids(pair, n))
            for n in range(TB):
                step(ids(MG // 2, n + 1) if n + 1 < TB else None, ids(MG // 2, n))

        block = ctx.enter_context(nc.Block())

        @block.sync
        def _(sp):
            sp.dma_start(x_raw[:, :, 0:N], xT[:, :, 0:N]).then_inc(x_loaded[0], 16)
            sp.dma_start(w_raw[:, :, :], w_qkv[0].rearrange("p (u n) -> p u n", u=3)).then_inc(w_loaded, 16)
            sp.dma_start(x_raw[:, :, N:T], xT[:, :, N:T]).then_inc(x_loaded[1], 16)
            sp.dma_start(mask_sb[:, :, :], masks).then_inc(consts_loaded, 16)
            sp.dma_start(ident[:, :], identity).then_inc(consts_loaded, 16)
            sp.dma_start(wo_raw, w_o[0]).then_inc(wo_loaded, 16)

            def load_codes(f):
                sp.dma_start(code_sb[:, :], codes[bass.ds(f, 1), :, :].rearrange("a p c -> (a p) c")).then_inc(codes_loaded, 16)

            def load_absmax(f):
                for half in range(2):
                    sp.dma_start(absmax_sb[64 * half:64 * half + 64, :],
                                 absmax[bass.ds(f, 1), half, :].broadcast_to([64, CW])).then_inc(absmax_loaded, 16)

            def park(f):
                sp.wait_ge(w_split_ready, f + 1)
                sp.dma_start(parked[:, :, bass.ds(f * CW, CW)], w_split).then_inc(parked_sem, 16)

            load_codes(0)
            load_absmax(0)
            sp.wait_ge(x_lo, B)
            sp.dma_start(acc[:, :, :], x.rearrange("(t p) d -> p t d", p=P)).then_inc(acc_loaded, 16)
            with sp.Fori(0, CHUNKS - 1) as f:
                sp.wait_ge(bits_ready, f + 1)
                load_codes(f + 1)
                sp.wait_ge(absmax_used, f + 1)
                load_absmax(f + 1)
                park(f)
            park(CHUNKS - 1)
            for tb in range(TB):
                sp.wait_ge(out_normed, 4 * (tb + 1))
                sp.dma_start(out.rearrange("(t p) d -> p t d", p=P)[:, 4 * tb:4 * tb + 4, :],
                             acc[:, 4 * tb:4 * tb + 4, :]).then_inc(out_stored, 16)
            sp.wait_ge(out_stored, 16 * TB)

        @block.gpsimd
        def _(pool):
            def step(front, b, back, back_b, back_g, new_group):
                if back is not None:
                    pool.wait_ge(merged, back * 3 + 3)
                    pool.wait_ge(absmax_loaded, back * 32 + 32)
                    nc.gpsimd.tensor_tensor(w_scaled, w_value, absmax_sb[:, :], ALU.mult)
                    nc.gpsimd.tensor_tensor(w_split[:, HI, :].bitcast(F32R), w_value, absmax_sb[:, :],
                                            ALU.mult).then_inc(absmax_used, 1)
                    pool.wait_ge(absmax_used, back + 1)
                    nc.gpsimd.tensor_tensor(w_split[:, LO, :].bitcast(F32R), w_scaled, w_split[:, HI, :],
                                            ALU.subtract).then_inc(w_split_ready, 1)
                if front is not None:
                    for c in range(2):
                        pool.wait_ge(inv_ready, front * 2 + c + 1)
                        tiles = probs[:, c, :].rearrange("p (j m) -> p j m", j=NB)
                        nc.gpsimd.tensor_tensor(tiles, tiles, row_inv[:, c, :].unsqueeze(2).to_broadcast([P, NB, P]),
                                                ALU.mult).then_inc(probs_ready, 1)

            step(0, 0, None, None, None, 0)
            attention_steps(pool, step)

        @block.tensor
        def _(pe):
            def project(dst, unit, col, b, last_sem):
                for k in range(KT):
                    for n, (s, m) in enumerate(PASSES):
                        mm = nc.tensor.matmul(dst, w_parts[:, s, unit, k, col:col + P],
                                              x_parts[:, m, k, bass.ds(b * N, N)],
                                              start=(k == 0 and n == 0), stop=(k == KT - 1 and n == 2))
                if last_sem is not None:
                    mm.then_inc(last_sem, 1)

            def step(front, b, back, back_b, back_g, new_group):
                if front is not None:
                    for c in range(2):
                        if new_group is not None:
                            pe.wait_ge(w_lo, new_group * 3 + c + 1)
                        if new_group is not None and isinstance(front, int):
                            pe.wait_ge(x_lo, 1)
                        if back is not None:
                            pe.wait_ge(k_lo if c == 0 else v_lo, front)
                            if c == 0:
                                pe.wait_ge(x_lo, b + 1)
                        for h in range(2):
                            project(PROJ[c][:, h * N:(h + 1) * N], c, h * P, b, q_done if h else None)
                if back is not None:
                    for c in range(2):
                        pe.wait_ge(probs_ready, back * 2 + c + 1)
                    if isinstance(front, int) or back is not None:
                        pe.wait_ge(consts_loaded, 32)
                    for bp in range(2):
                        for j in (2 * bp, 2 * bp + 1):
                            for c in range(2):
                                at_ = (j % 2) * 256 + c * P
                                mm = nc.tensor.transpose(TURN[bp][:, at_:at_ + P],
                                                         probs[:, c, j * P:(j + 1) * P], ident[:, :])
                        mm.then_inc(probs_turned, 1)
                if front is not None:
                    if new_group is not None:
                        pe.wait_ge(w_lo, new_group * 3 + 3)
                    pe.wait_ge(q_lo, front * 2 + 1)
                    for h in range(2):
                        project(PROJ[0][:, h * N:(h + 1) * N], 2, h * P, b, kv_done if h else None)
                if back is not None:
                    for bp in range(2):
                        pe.wait_ge(pt_lo, back * 2 + bp + 1)
                        pe.wait_ge(y_added, back * 2 + 1 + bp)
                        if bp == 0:
                            runs = ((0, 512, WINDOW[0]),)
                        else:
                            runs = ((0, 256, WINDOW[2]), (256, 512, WINDOW[3]))
                        for lo_, hi_, w in runs:
                            for n, (s, m) in enumerate(PASSES):
                                mm = nc.tensor.matmul(CTX[bp][:, lo_:hi_], v_parts[:, s, w, :],
                                                      pt_parts[:, m, bp, lo_:hi_],
                                                      start=(n == 0), stop=(n == 2))
                        mm.then_inc(ctx_done, 1)
                if front is not None:
                    pe.wait_ge(vT_copied, front + 1)
                    pe.wait_ge(q_lo, front * 2 + 2)
                    if isinstance(front, int):
                        pe.wait_ge(consts_loaded, 32)
                    for w in range(3):
                        mm = nc.tensor.transpose(PROJ[1][:, w * P:(w + 1) * P],
                                                 vT[:, w * QB:w * QB + P], ident[:, :])
                    mm.then_inc(v_turned, 1)
                    pe.wait_ge(k_lo, front + 1)
                    for c in range(2):
                        for j in range(NB):
                            ws = WINDOW_START[j]
                            for n, (s, m) in enumerate(PASSES):
                                mm = nc.tensor.matmul(SCORE[c][:, j * P:(j + 1) * P], q_parts[:, s, c, j, :],
                                                      k_parts[:, m, ws:ws + P], start=(n == 0), stop=(n == 2))
                        mm.then_inc(scores_done, 1)
                if back is not None:
                    pe.wait_ge(wo_lo, back_g + 1)
                    for tt in range(2):
                        pe.wait_ge(o_lo, back * 2 + tt + 1)
                        for h in range(HQ):
                            for n, (s, m) in enumerate(PASSES):
                                mm = nc.tensor.matmul(CTX[tt][:, 0:D], o_parts[:, s, h, tt * P:(tt + 1) * P],
                                                      wo_parts[:, m, h, :], start=(h == 0 and n == 0),
                                                      stop=(h == HQ - 1 and n == 2))
                        mm.then_inc(y_done, 1)

            step(0, 0, None, None, None, 0)
            attention_steps(pe, step)

            for t in range(TT):
                pe.wait_ge(x1_normed, t + 1)
                if t >= 2:
                    pe.wait_ge(x1_lo, t - 1)
                for k in range(KT):
                    mm = nc.tensor.transpose(PROJ[t % 2][:, k * P:(k + 1) * P],
                                             acc[:, t, k * P:(k + 1) * P], ident[:, :])
                mm.then_inc(x1_turned, 1)

            GU, DOWN = bank[0:4], bank[4:8]

            def ffn(front, back):
                if front is not None:
                    s, mg, half, tb, wbuf, hbuf = front
                    if tb == 0:
                        pe.wait_ge(ffn_loaded[wbuf], (half + 1) * 16)
                    if back is None:
                        pe.wait_ge(x1_lo, TT)
                    for c in range(2):
                        if back is not None:
                            pe.wait_ge(hid_ready, (s - 1) * 2 + c + 1)
                        for kind in range(2):
                            for k in range(KT):
                                i = kind * 2 + k // 2
                                col = (k % 2) * 256 + c * P
                                for n, (st, mv) in enumerate(PASSES):
                                    mm = nc.tensor.matmul(GU[2 * c + kind][:, :],
                                                          ffn_w[wbuf][:, st, i, col:col + P],
                                                          x_parts[:, mv, k, tb * 512:(tb + 1) * 512],
                                                          start=(k == 0 and n == 0),
                                                          stop=(k == KT - 1 and n == 2))
                        mm.then_inc(gu_done, 1)
                if back is not None:
                    s, mg, half, tb, wbuf, hbuf = back
                    for c in range(2):
                        pe.wait_ge(hid_lo, s * 2 + c + 1)
                    for tt in range(4):
                        pe.wait_ge(y_added, s * 4 + (2 * G * B - 1) + tt)
                        for c in range(2):
                            for n, (st, mv) in enumerate(PASSES):
                                mm = nc.tensor.matmul(DOWN[tt][:, :], hid[hbuf][:, st, c, tt * P:(tt + 1) * P],
                                                      ffn_w[wbuf][:, mv, 4 + c, :],
                                                      start=(c == 0 and n == 0), stop=(c == 1 and n == 2))
                        mm.then_inc(down_done, 1)

            ffn_steps(pe, ffn)

        @block.scalar
        def _(act):
            def copy(dst, src):
                return nc.scalar.activation(dst, src, ACT.Copy)

            def step(front, b, back, back_b, back_g, new_group):
                if new_group is not None:
                    act.wait_ge(w_loaded, new_group * 16 + 16)
                    if back is not None:
                        act.wait_ge(kv_done, front)
                    for u in range(3):
                        copy(w_parts[:, HI, u, :, :], w_raw[:, u, :].rearrange("p (k c) -> p k c", k=KT)).then_inc(w_hi, 1)
                if front is not None:
                    for c in range(2):
                        act.wait_ge(q_done, front * 2 + c + 1)
                        copy(q_parts[:, HI, c, :, :].rearrange("p j (h q) -> p j h q", h=2),
                             PROJ[c][:, :].rearrange("p (h j q) -> p j h q", h=2, j=NB)).then_inc(q_hi, 1)
                if back is not None:
                    for bp in range(2):
                        act.wait_ge(probs_turned, back * 2 + bp + 1)
                        copy(pt_parts[:, HI, bp, :], TURN[bp][:, :]).then_inc(pt_hi, 1)
                if front is not None:
                    act.wait_ge(kv_done, front + 1)
                    copy(vT[:, :], PROJ[0][:, N:2 * N]).then_inc(vT_copied, 1)
                    copy(k_parts[:, HI, :], PROJ[0][:, 0:N]).then_inc(k_hi, 1)
                if back is not None:
                    for bp in range(2):
                        act.wait_ge(ctx_done, back * 2 + bp + 1)
                        copy(o_parts[:, HI, :, bp * P:(bp + 1) * P].rearrange("p h (k q) -> p k h q", k=2),
                             CTX[bp][:, :].rearrange("p (k h q) -> p k h q", k=2, h=HQ)).then_inc(o_hi, 1)
                if front is not None:
                    act.wait_ge(v_turned, front + 1)
                    copy(v_parts[:, HI, :, :].rearrange("p w d -> p (w d)"), PROJ[1][:, 0:3 * P]).then_inc(v_hi, 1)
                    for c in range(2):
                        act.wait_ge(neg_max_ready, front * 2 + c + 1)
                        for j in range(NB):
                            at_ = probs[:, c, j * P:(j + 1) * P]
                            e = nc.scalar.activation(at_, at_, ACT.Exp, bias=neg_max[:, c, j:j + 1], scale=SCALE,
                                                     accum_out=row_sum[:, c, j:j + 1])
                        e.then_inc(exp_done, 1)
                    act.wait_ge(bits_ready, front + 1)
                    if back is not None:
                        act.wait_ge(parked_sem, front * 16)
                    for k, (base, slope) in enumerate(code_lines()):
                        pair = nc.scalar.activation(pair_value[:, k, :], code_bits[:, 0, :], ACT.Copy,
                                                    bias=base, scale=slope)
                    pair.then_inc(pairs_ready, 1)
                if new_group is not None:
                    act.wait_ge(wo_loaded, new_group * 16 + 16)
                    if back is not None:
                        act.wait_ge(y_done, back * 2 + 2)
                    copy(wo_parts[:, HI, :, :].rearrange("p h d -> p (h d)"), wo_raw).then_inc(wo_hi, 1)

            def split_x(b):
                act.wait_ge(x_loaded[min(b, 1)], 16)
                copy(x_parts[:, HI, :, b * N:(b + 1) * N], x_raw[:, :, b * N:(b + 1) * N]).then_inc(x_hi, 1)

            def next_weights(g):
                act.wait_ge(w_lo, g * 3 + 3)
                act.dma_start(w_raw, w_qkv[bass.ds(g + 1, 1), :, :].rearrange("g p (u n) -> (g p) u n", u=3)).then_inc(w_loaded, 16)
                act.wait_ge(wo_lo, g + 1)
                act.dma_start(wo_raw, w_o[bass.ds(g + 1, 1), :, :].rearrange("g p n -> (g p) n")).then_inc(wo_loaded, 16)

            split_x(0)
            step(0, 0, None, None, None, 0)
            for b in range(1, B):
                split_x(b)
            attention_steps(act, step, next_weights)

            def load_ffn(mg, wbuf):
                act.dma_start(f32(ffn_w[wbuf]).rearrange("p s i c -> p s (i c)"),
                              parked[:, :, bass.ds(mg * GC, GC)]).then_inc(ffn_loaded[wbuf], 16)

            act.wait_ge(y_done, 2 * G * B)
            act.wait_ge(parked_sem, 16 * CHUNKS)
            load_ffn(0, 0)

            def std(n, lo_, hi_):
                act.wait_ge(var_done, n + 1)
                if n == 0:
                    act.wait_ge(eps_set, 1)
                nc.scalar.activation(rstd[:, lo_:hi_], mean_var[:, lo_:hi_, 1:2].rearrange("p t a -> p (t a)"),
                                     ACT.Sqrt, bias=eps_sb[:, 0:1]).then_inc(std_done, 1)

            std(0, 0, TT)
            for t in range(TT):
                act.wait_ge(x1_turned, t + 1)
                copy(x_parts[:, HI, :, t * P:(t + 1) * P],
                     PROJ[t % 2][:, :].rearrange("p (k t) -> p k t", k=KT)).then_inc(x1_hi, 1)

            def ffn(front, back):
                if front is not None:
                    s, mg, half, tb, wbuf, hbuf = front
                    if tb == 1 and not (isinstance(mg, int) and mg == MG - 1):
                        act.wait_ge(gu_done, s * 2 + 1)
                        load_ffn(mg + 1, 1 - wbuf)
                    for c in range(2):
                        act.wait_ge(gu_done, s * 2 + c + 1)
                        if back is not None:
                            act.wait_ge(hid_ready, (s - 1) * 2 + c + 1)
                        nc.scalar.activation(silu_g[:, c, :], bank[2 * c][:, :], ACT.Silu).then_inc(silu_done, 1)
                    for c in range(2):
                        act.wait_ge(hid_ready, s * 2 + c + 1)
                        copy(hid[hbuf][:, HI, c, :], hid_f[:, c, :]).then_inc(hid_hi, 1)
                if back is not None and isinstance(back[1], int) and back[1] == MG - 1:
                    tb = back[3]
                    std(1 + tb, 4 * tb, 4 * tb + 4)

            ffn_steps(act, ffn)

        @block.vector
        def _(dve):
            def low(dst, src, hi):
                return nc.vector.tensor_tensor(dst, src, f32(hi), ALU.subtract)

            def merge(level):
                view = pair_value[:, :, :].rearrange("p (j a) c -> p j a c", a=1 << level)
                nc.vector.copy_predicated(view[:, :, 0, :], bit_mask(level, 8 >> level),
                                          view[:, :, 1 << (level - 1), :]).then_inc(merged, 1)

            def bit_mask(bit, times):
                return code_bits[:, bit:bit + 1, :].broadcast_to([P, times, CW])

            def take_bits(f):
                codes_u8 = code_sb[:, :].bitcast(mybir.dt.uint8).rearrange("p (c e) -> p c e", e=4)[:, :, 0]
                if not isinstance(f, int):
                    dve.wait_ge(merged, f * 3)
                dve.wait_ge(codes_loaded, f * 16 + 16)
                for bit in range(4):
                    i = nc.vector.tensor_scalar(code_bits[:, bit, :], codes_u8, 1 << bit, None, ALU.bitwise_and)
                i.then_inc(bits_ready, 1)

            def step(front, b, back, back_b, back_g, new_group):
                if back is not None:
                    merge(1)
                if new_group is not None:
                    for u in range(3):
                        dve.wait_ge(w_hi, new_group * 3 + u + 1)
                        low(w_parts[:, LO, u, :, :], w_raw[:, u, :].rearrange("p (k c) -> p k c", k=KT),
                            w_parts[:, HI, u, :, :]).then_inc(w_lo, 1)
                if front is not None:
                    for c in range(2):
                        dve.wait_ge(q_hi, front * 2 + c + 1)
                        if back is not None:
                            dve.wait_ge(merged, back * 3 + c + 1)
                        low(q_parts[:, LO, c, :, :].rearrange("p j (h q) -> p j h q", h=2),
                            PROJ[c][:, :].rearrange("p (h j q) -> p j h q", h=2, j=NB),
                            q_parts[:, HI, c, :, :].rearrange("p j (h q) -> p j h q", h=2)).then_inc(q_lo, 1)
                        if back is not None:
                            merge(c + 2)
                if back is not None:
                    for bp in range(2):
                        dve.wait_ge(pt_hi, back * 2 + bp + 1)
                        if front is None:
                            dve.wait_ge(merged, back * 3 + bp + 1)
                        low(pt_parts[:, LO, bp, :], TURN[bp][:, :], pt_parts[:, HI, bp, :]).then_inc(pt_lo, 1)
                        if front is None:
                            merge(bp + 2)
                if front is not None:
                    dve.wait_ge(k_hi, front + 1)
                    low(k_parts[:, LO, :], PROJ[0][:, 0:N], k_parts[:, HI, :]).then_inc(k_lo, 1)
                if back is not None:
                    for bp in range(2):
                        dve.wait_ge(o_hi, back * 2 + bp + 1)
                        o_view = [o_parts[:, s, :, bp * P:(bp + 1) * P].rearrange("p h (k q) -> p k h q", k=2)
                                  for s in (HI, LO)]
                        low(o_view[LO], CTX[bp][:, :].rearrange("p (k h q) -> p k h q", k=2, h=HQ),
                            o_view[HI]).then_inc(o_lo, 1)
                if front is not None:
                    dve.wait_ge(v_hi, front + 1)
                    low(v_parts[:, LO, :, :].rearrange("p w d -> p (w d)"), PROJ[1][:, 0:3 * P],
                        v_parts[:, HI, :, :].rearrange("p w d -> p (w d)")).then_inc(v_lo, 1)
                    for c in range(2):
                        dve.wait_ge(consts_loaded, 32)
                        dve.wait_ge(scores_done, front * 2 + c + 1)
                        for j in range(NB):
                            m = nc.vector.tensor_tensor_reduce(
                                out=probs[:, c, j * P:(j + 1) * P], in0=SCORE[c][:, j * P:(j + 1) * P],
                                in1=mask_sb[:, min(j, 1), :], scale=1.0, scalar=-3.4e38, op0=ALU.add,
                                op1=ALU.max, accum_out=row_max[:, c, j:j + 1])
                        m.then_inc(max_found, 1)
                        dve.wait_ge(max_found, front * 2 + c + 1)
                        nc.vector.tensor_scalar(neg_max[:, c, :], row_max[:, c, :], -SCALE, None,
                                                ALU.mult).then_inc(neg_max_ready, 1)
                    take_bits(front)
                    for c in range(2):
                        dve.wait_ge(exp_done, front * 2 + c + 1)
                        nc.vector.reciprocal(row_inv[:, c, :], row_sum[:, c, :]).then_inc(inv_ready, 1)
                if back is not None:
                    for tt in range(2):
                        dve.wait_ge(y_done, back * 2 + tt + 1)
                        dve.wait_ge(acc_loaded, 16)
                        if front is not None and tt == 1:
                            dve.wait_ge(pairs_ready, front + 1)
                        row = acc[:, bass.ds(back_b * 2 + tt, 1), :].rearrange("p a d -> p (a d)")
                        nc.vector.tensor_tensor(row, CTX[tt][:, :], row, ALU.add).then_inc(y_added, 1)
                if new_group is not None:
                    dve.wait_ge(wo_hi, new_group + 1)
                    low(wo_parts[:, LO, :, :].rearrange("p h d -> p (h d)"), wo_raw,
                        wo_parts[:, HI, :, :].rearrange("p h d -> p (h d)")).then_inc(wo_lo, 1)

            def split_x(b):
                dve.wait_ge(x_hi, b + 1)
                low(x_parts[:, LO, :, b * N:(b + 1) * N], x_raw[:, :, b * N:(b + 1) * N],
                    x_parts[:, HI, :, b * N:(b + 1) * N]).then_inc(x_lo, 1)

            nc.vector.memset(eps_sb[:, :], LN_EPS).then_inc(eps_set, 1)
            nc.vector.memset(row_max[:, :, :], 0.0).then_inc(y_added, 2)
            split_x(0)
            step(0, 0, None, None, None, 0)
            dve.wait_ge(pairs_ready, 1)
            for b in range(1, B):
                split_x(b)
            attention_steps(dve, step)

            def variances(n, lo_, hi_):
                dve.wait_ge(y_added, last_added[0])
                for t in range(lo_, hi_):
                    i = nc.vector.bn_stats(stats[:, t, :], acc[:, t, :])
                i.then_inc(stats_done, 1)
                dve.wait_ge(stats_done, n + 1)
                for t in range(lo_, hi_):
                    i = nc.vector.bn_aggr(mean_var[:, t, :], stats[:, t, :])
                i.then_inc(var_done, 1)
                dve.wait_ge(std_done, n + 1)
                nc.vector.reciprocal(rstd[:, lo_:hi_], rstd[:, lo_:hi_]).then_inc(rstd_done, 1)
                dve.wait_ge(rstd_done, n + 1)

            def norm(t):
                return nc.vector.tensor_scalar(acc[:, t, :], acc[:, t, :], mean_var[:, t, 0:1], rstd[:, t:t + 1],
                                               ALU.subtract, ALU.mult)

            last_added = [2 * G * B + 2]
            variances(0, 0, TT)
            norm(0).then_inc(x1_normed, 1)
            for t in range(TT):
                if t + 1 < TT:
                    norm(t + 1).then_inc(x1_normed, 1)
                dve.wait_ge(x1_hi, t + 1)
                low(x_parts[:, LO, :, t * P:(t + 1) * P], PROJ[t % 2][:, :].rearrange("p (k t) -> p k t", k=KT),
                    x_parts[:, HI, :, t * P:(t + 1) * P]).then_inc(x1_lo, 1)

            def ffn(front, back):
                if front is not None:
                    s, mg, half, tb, wbuf, hbuf = front
                    for c in range(2):
                        dve.wait_ge(silu_done, s * 2 + c + 1)
                        if back is not None:
                            dve.wait_ge(hid_lo, (s - 1) * 2 + c + 1)
                        nc.vector.tensor_tensor(hid_f[:, c, :], bank[2 * c + 1][:, :], silu_g[:, c, :],
                                                ALU.mult).then_inc(hid_ready, 1)
                    for c in range(2):
                        dve.wait_ge(hid_hi, s * 2 + c + 1)
                        low(hid[hbuf][:, LO, c, :], hid_f[:, c, :], hid[hbuf][:, HI, c, :]).then_inc(hid_lo, 1)
                if back is not None:
                    s, mg, half, tb, wbuf, hbuf = back
                    for tt in range(4):
                        dve.wait_ge(down_done, s * 4 + tt + 1)
                        row = acc[:, tb * 4 + tt, :]
                        nc.vector.tensor_tensor(row, bank[4 + tt][:, :], row, ALU.add).then_inc(y_added, 1)
                    if isinstance(mg, int) and mg == MG - 1:
                        last_added[0] = 2 * G * B + 4 * s + 6
                        variances(1 + tb, tb * 4, tb * 4 + 4)
                        for tt in range(4):
                            norm(tb * 4 + tt).then_inc(out_normed, 1)

            ffn_steps(dve, ffn)


def kernel(L0_attn_x, L0_attn_wq, L0_attn_wk, L0_attn_wv, L0_attn_wo, L0_ffn_gate_q, L0_ffn_gate_absmax,
           L0_ffn_up_q, L0_ffn_up_absmax, L0_ffn_down_q, L0_ffn_down_absmax):
    import concourse.bacc as bacc
    from concourse.bass_utils import run_bass_kernel_spmd

    x, wq, wk, wv, wo = (np.asarray(a) for a in (L0_attn_x, L0_attn_wq, L0_attn_wk, L0_attn_wv, L0_attn_wo))
    B, N, D = x.shape
    T, KT, G = B * N, D // P, wk.shape[0] // P
    HQ = wq.shape[0] // P // G
    M = np.asarray(L0_ffn_gate_q).shape[0]
    MG = M // 256

    tokens = x.reshape(T, D)
    xT = tokens.T.reshape(KT, P, T).transpose(1, 0, 2)
    heads = np.concatenate([wq.reshape(G, HQ, P, D), wk.reshape(G, 1, P, D), wv.reshape(G, 1, P, D)], axis=1)
    w_qkv = heads.reshape(G, 3, 256, KT, P).transpose(0, 4, 1, 3, 2).reshape(G, P, -1)
    w_o = wo.reshape(D, G, HQ, P).transpose(1, 3, 2, 0).reshape(G, P, -1)

    def up_chunks(q, absmax):
        q = np.asarray(q).reshape(MG, 256, 2, 2, P).transpose(0, 2, 4, 3, 1).reshape(MG, 2, P, 512)
        a = np.asarray(absmax).reshape(MG, 256, 2, 2, 2).transpose(0, 2, 4, 3, 1).reshape(MG, 2, 2, 512)
        return q, a

    def down_chunks(q, absmax):
        q = np.asarray(q).reshape(D, MG, 2, P).transpose(1, 2, 3, 0)
        a = np.asarray(absmax).reshape(D, MG, 2, 2).transpose(1, 2, 3, 0)
        return q, a

    parts = [up_chunks(L0_ffn_gate_q, L0_ffn_gate_absmax), up_chunks(L0_ffn_up_q, L0_ffn_up_absmax),
             down_chunks(L0_ffn_down_q, L0_ffn_down_absmax)]
    codes, absmax = (np.concatenate([p[n] for p in parts], axis=1) for n in range(2))
    codes = codes.transpose(2, 0, 1, 3).reshape(P, G * B, -1).transpose(1, 0, 2)
    absmax = absmax.transpose(2, 0, 1, 3).reshape(2, G * B, -1).transpose(1, 0, 2)

    i, m = np.arange(P)[:, None] % 64, np.arange(P)[None, :]
    first = np.where(m <= i, 0.0, MASKED)
    later = np.where((m > i) & (m <= i + 64), 0.0, MASKED)
    masks = np.stack([first, later], axis=1).astype(np.float32)

    nc = bacc.Bacc("TRN2", target_bir_lowering=False, num_devices=1)
    arrays, ins = {}, []
    for name, a in (("x", tokens), ("xT", xT), ("w_qkv", w_qkv), ("w_o", w_o), ("codes", codes),
                    ("absmax", absmax), ("masks", masks), ("identity", np.eye(P, dtype=np.float32))):
        a = np.ascontiguousarray(a)
        arrays[name] = a
        ins.append(nc.dram_tensor(name, a.shape, mybir.dt.from_np(a.dtype), kind="ExternalInput").ap())
    out = nc.dram_tensor("out", (T, D), F32, kind="ExternalOutput").ap()
    decoder_layer(nc, *ins, out)
    r = run_bass_kernel_spmd(nc, [arrays], core_ids=[0])
    return np.asarray(r.results[0]["out"]).reshape(B, N, D)
```

```python
from contextlib import ExitStack

import numpy as np

import concourse.bass as bass
from concourse import mybir

F32 = mybir.dt.float32
F32R = mybir.dt.float32r
ALU = mybir.AluOpType
ACT = mybir.ActivationFunctionType

P = 128
NF4_CODE = [-1.0, -0.6961928009986877, -0.5250730514526367, -0.39491748809814453,
            -0.28444138169288635, -0.18477343022823334, -0.09105003625154495, 0.0,
            0.07958029955625534, 0.16093020141124725, 0.24611230194568634, 0.33791524171829224,
            0.44070982933044434, 0.5626170039176941, 0.7229568362236023, 1.0]


def code_lines():
    lines = []
    for k in range(0, len(NF4_CODE), 2):
        base, top = np.float32(NF4_CODE[k]), np.float32(NF4_CODE[k + 1])
        slope = np.float32(top - base)
        for s in (slope, np.nextafter(slope, np.float32(9)), np.nextafter(slope, np.float32(-9))):
            if np.float32(base + s) == top:
                lines.append((float(base), float(s)))
                break
    assert len(lines) == len(NF4_CODE) // 2
    return lines


MASKED = -3.0e38
LN_EPS = 1e-5
HI, LO = 0, 1
PASSES = ((HI, HI), (HI, LO), (LO, HI))


def decoder_layer(nc, x, xT, w_qkv, w_o, codes, absmax, masks, identity, out):
    _, KT, T = xT.shape
    G, _, _ = w_qkv.shape
    D = KT * P
    N = 256
    B = T // N
    HQ = 4
    QB = 64
    NB = N // QB
    GC = 6 * 512
    CHUNKS, _, CW = codes.shape
    MG = CHUNKS * CW // GC
    TB = T // 512
    TT = T // P
    SCALE = float(P) ** -0.5
    WINDOW_START = (0, 0, QB, 2 * QB)
    WINDOW = (0, 0, 1, 2)
    assert N == 256 and HQ == 4 and NB == 4 and CHUNKS == G * B and MG % 2 == 1 and T % 512 == 0

    ctx = ExitStack()
    with ctx:
        def sb(name, shape, dt=F32):
            return ctx.enter_context(nc.sbuf_tensor(name, shape, dt))

        def sem(name):
            return ctx.enter_context(nc.semaphore(name))

        parked = nc.dram_tensor("ffn_parts", [P, 2, MG * GC], F32, kind="Internal").ap()

        x_parts = sb("x_parts", [P, 2, KT, T], F32R)
        acc = sb("acc", [P, TT, D])
        x_raw = acc[:, :, :].rearrange("p t d -> p (t d)").rearrange("p (b k n) -> p b k n", b=B, k=KT)
        UW = KT * 256
        HALF = KT // 2
        EARLY = 3
        LATE = B // 2 + 1
        sizes = [2 * 3 * UW, 2 * HQ * D, 2 * HQ * N, 2 * N, 2 * 3 * P, 2 * HQ * N, 2 * HQ * N]
        rounded = sb("rounded", [P, sum(sizes)], F32R)
        at = [sum(sizes[:n]) for n in range(len(sizes))]

        def part(n):
            return rounded[:, at[n]:at[n] + sizes[n]]

        w_parts = part(0).rearrange("p (s u k c) -> p s u k c", s=2, u=3, k=KT)
        wo_parts = part(1).rearrange("p (s h d) -> p s h d", s=2, h=HQ)
        q_parts = part(2).rearrange("p (s c j m) -> p s c j m", s=2, c=2, j=NB)
        k_parts = part(3).rearrange("p (s t) -> p s t", s=2)
        v_parts = part(4).rearrange("p (s w d) -> p s w d", s=2, w=3)
        pt_parts = part(5).rearrange("p (s b m) -> p s b m", s=2, b=2)
        o_parts = part(6).rearrange("p (s h t) -> p s h t", s=2, h=HQ)
        ffn_w = [rounded[:, n * 2 * GC:(n + 1) * 2 * GC].rearrange("p (s i c) -> p s i c", s=2, i=6)
                 for n in range(2)]
        hid = [rounded[:, 4 * GC + n * 2048:4 * GC + (n + 1) * 2048]
               .rearrange("p (s c t) -> p s c t", s=2, c=2) for n in range(2)]
        raw = sb("raw", [P, 3 * UW + HQ * D])
        w_raw = raw[:, 0:3 * UW].rearrange("p (u n) -> p u n", u=3)
        wo_raw = raw[:, 3 * UW:3 * UW + HQ * D]
        silu_g = raw[:, 0:1024].rearrange("p (c t) -> p c t", c=2)
        hid_f = raw[:, 1024:2048].rearrange("p (c t) -> p c t", c=2)
        vT = sb("vT", [P, N])
        probs = sb("probs", [P, 2, NB * P])
        mask_sb = sb("mask_sb", [P, NB, P])
        ident = sb("ident", [P, P])
        row_max = sb("row_max", [P, 2, NB])
        neg_max = sb("neg_max", [P, 2, NB])
        row_sum = sb("row_sum", [P, 2, NB])
        row_inv = sb("row_inv", [P, 2, NB])
        stats = sb("stats", [P, TT, 6])
        mean_var = sb("mean_var", [P, TT, 2])
        rstd = sb("rstd", [P, TT])
        eps_sb = sb("eps_sb", [P, 1])
        ones = sb("ones", [P, 1])
        code_sb = sb("code_sb", [P, CW], mybir.dt.int32)
        code_bits = sb("code_bits", [P, 4, CW], mybir.dt.uint8)
        absmax_sb = sb("absmax_sb", [P, CW])
        pair_value = sb("pair_value", [P, 8, CW])
        w_value, w_scaled, w_split = pair_value[:, 0, :], pair_value[:, 1, :], pair_value[:, 2:4, :]

        PROJ = [ctx.enter_context(nc.psum_tensor(f"proj{n}", [P, 512], F32)) for n in range(2)]
        middle = ctx.enter_context(nc.psum_tensor("middle", [P, 4, 512], F32))
        CTX = [ctx.enter_context(nc.psum_tensor(f"ctx{n}", [P, 512], F32)) for n in range(2)]
        score = middle[:, :, :].rearrange("p (c b) (j s m) -> p c (b j) s m", c=2, j=2, s=2)
        TURN = [middle[:, 2 + n, :] for n in range(2)]
        bank = [PROJ[0][:, :], PROJ[1][:, :]] + [middle[:, n, :] for n in range(4)] + [CTX[0][:, :], CTX[1][:, :]]

        x_half_loaded, w_half_loaded = sem("x_half_loaded"), sem("w_half_loaded")
        x_loaded = [sem(f"x_loaded{b}") for b in range(B)]
        acc_loaded = sem("acc_loaded")
        consts_loaded = sem("consts_loaded")
        w_loaded, wo_loaded = [sem(f"w_loaded{u}") for u in range(3)], sem("wo_loaded")
        codes_loaded, absmax_loaded = sem("codes_loaded"), sem("absmax_loaded")
        parked_sem = sem("parked")
        ffn_loaded = [sem("ffn_loaded0"), sem("ffn_loaded1")]
        out_stored = sem("out_stored")
        wo_hi, wo_lo, probs_ready = sem("wo_hi"), sem("wo_lo"), sem("probs_ready")
        x_late_hi = sem("x_late_hi")
        absmax_used, w_split_ready = sem("absmax_used"), sem("w_split_ready")
        out_normed_too = sem("out_normed_too")
        q_done, kv_done, v_turned = sem("q_done"), sem("kv_done"), sem("v_turned")
        scores_done, probs_turned = sem("scores_done"), sem("probs_turned")
        ctx_done, y_done = sem("ctx_done"), sem("y_done")
        x1_turned, gu_done, down_done = sem("x1_turned"), sem("gu_done"), sem("down_done")
        x0_hi, x_hi, w_half_hi, w_hi = sem("x0_hi"), sem("x_hi"), sem("w_half_hi"), sem("w_hi")
        q_hi, k_hi, v_hi, vT_copied = sem("q_hi"), sem("k_hi"), sem("v_hi"), sem("vT_copied")
        exp_done, pt_hi, o_hi = sem("exp_done"), sem("pt_hi"), sem("o_hi")
        std_done, x1_hi = sem("std_done"), sem("x1_hi")
        pairs_ready = sem("pairs_ready")
        silu_done, hid_hi = sem("silu_done"), sem("hid_hi")
        x0_lo, x1st_hi, x_lo = sem("x0_lo"), sem("x1st_hi"), sem("x_lo")
        w_half_lo, w_lo, ones_set = sem("w_half_lo"), sem("w_lo"), sem("ones_set")
        q_lo, k_lo, v_lo = sem("q_lo"), sem("k_lo"), sem("v_lo")
        masked = sem("masked")
        max_found, neg_max_ready, inv_ready = sem("max_found"), sem("neg_max_ready"), sem("inv_ready")
        bits_ready, merged = sem("bits_ready"), sem("merged")
        pt_lo, o_lo, y_added = sem("pt_lo"), sem("o_lo"), sem("y_added")
        eps_set, stats_done, var_done, rstd_done, x1_normed, x1_lo = (
            sem("eps_set"), sem("stats_done"), sem("var_done"), sem("rstd_done"), sem("x1_normed"),
            sem("x1_lo"))
        hid_ready, hid_lo = sem("hid_ready"), sem("hid_lo")
        out_normed, last_normed = sem("out_normed"), sem("last_normed")

        def f32(ap):
            return ap.bitcast(F32)

        def attention_steps(eng, step):
            with eng.Fori(0, G - 1) as g:
                with eng.Fori(1, B - 1) as b:
                    step(g * B + b, b, g * B + b - 1, b - 1, g)
                step(g * B + (B - 1), B - 1, g * B + (B - 2), B - 2, g, w_next=g + 1)
                step(g * B + B, 0, g * B + (B - 1), B - 1, g, first_of=g + 1)
            with eng.Fori(1, B - 1) as b:
                step((G - 1) * B + b, b, (G - 1) * B + b - 1, b - 1, G - 1, last=True)
            step(G * B - 1, B - 1, G * B - 2, B - 2, G - 1, last=True, ending=True)
            step(None, None, G * B - 1, B - 1, G - 1, last=True)

        def ffn_steps(eng, step):
            def ids(pair, n):
                mg = n // TB
                return pair * (2 * TB) + n, pair * 2 + mg, pair + mg // 2, n % TB, mg % 2, n % 2

            step(ids(0, 0), None)
            with eng.Fori(0, MG // 2) as pair:
                for n in range(2 * TB):
                    step(ids(pair, n + 1), ids(pair, n))
            for n in range(TB):
                step(ids(MG // 2, n + 1) if n + 1 < TB else None, ids(MG // 2, n))

        assert TB == 4
        NORM_RANGES = ([(0, 4), (4, TT - 2), (TT - 2, TT)] + [(4 * tb, 4 * tb + 4) for tb in range(TB - 1)]
                       + [(TT - 4, TT - 2), (TT - 2, TT)])

        def x1_bank(t):
            return bank[t if t < 4 else 4 + t % 4]

        def tiles_turned(c, kind):
            n = 2 * c + kind + 1
            return range(4 * n, 4 * n + 4) if n < TB else ()

        block = ctx.enter_context(nc.Block())

        @block.sync
        def _(sp):
            w_group0 = w_qkv[0].rearrange("p (u n) -> p u n", u=3)
            sp.dma_start(x_raw[:, 0, :HALF, :], xT[:, :HALF, 0:N]).then_inc(x_half_loaded, 16)
            sp.dma_start(w_raw[:, 0, 0:UW // 2], w_group0[:, 0, 0:UW // 2]).then_inc(w_half_loaded, 16)
            sp.dma_start(x_raw[:, 0, HALF:, :], xT[:, HALF:, 0:N]).then_inc(x_loaded[0], 16)
            sp.dma_start(w_raw[:, 0, UW // 2:], w_group0[:, 0, UW // 2:]).then_inc(w_loaded[0], 16)
            for u in range(1, 3):
                sp.dma_start(w_raw[:, u, :], w_group0[:, u, :]).then_inc(w_loaded[u], 16)
            sp.dma_start(ident[:, :], identity).then_inc(consts_loaded, 16)
            sp.dma_start(mask_sb[:, :, :], masks).then_inc(consts_loaded, 16)
            sp.dma_start(wo_raw, w_o[0]).then_inc(wo_loaded, 16)
            for b in range(1, B):
                sp.dma_start(x_raw[:, b, :, :], xT[:, :, b * N:(b + 1) * N]).then_inc(x_loaded[b], 16)

            def load_codes(f):
                sp.dma_start(code_sb[:, :], codes[bass.ds(f, 1), :, :].rearrange("a p c -> (a p) c")).then_inc(codes_loaded, 16)

            def load_absmax(f):
                for half in range(2):
                    sp.dma_start(absmax_sb[64 * half:64 * half + 64, :],
                                 absmax[bass.ds(f, 1), half, :].broadcast_to([64, CW])).then_inc(absmax_loaded, 16)

            def park(f):
                sp.wait_ge(w_split_ready, f + 1)
                sp.dma_start(parked[:, :, bass.ds(f * CW, CW)], w_split).then_inc(parked_sem, 16)

            load_codes(0)
            load_absmax(0)
            sp.wait_ge(bits_ready, 1)
            load_codes(1)
            sp.wait_ge(x0_lo, 2)
            for first, end in ((0, LATE), (LATE, B)):
                sp.wait_ge(x_lo, end - 1)
                tiles = slice(first * N // P, end * N // P)
                sp.dma_start(acc[:, tiles, :], x.rearrange("(t p) d -> p t d", p=P)[:, tiles, :]).then_inc(acc_loaded, 16)

            def chunk_traffic(f, codes_left=True):
                sp.wait_ge(absmax_used, f + 1)
                load_absmax(f + 1)
                park(f)
                if codes_left:
                    sp.wait_ge(bits_ready, f + 2)
                    load_codes(f + 2)

            with sp.Fori(0, G - 1) as g:
                chunk_traffic(g * B)
                sp.wait_ge(w_lo, g * 3 + 3)
                w_group = w_qkv[bass.ds(g + 1, 1), :, :].rearrange("g p (u n) -> (g p) u n", u=3)
                for u in range(3):
                    sp.dma_start(w_raw[:, u, :], w_group[:, u, :]).then_inc(w_loaded[u], 16)
                sp.wait_ge(wo_lo, g + 1)
                sp.dma_start(wo_raw, w_o[bass.ds(g + 1, 1), :, :].rearrange("g p n -> (g p) n")).then_inc(wo_loaded, 16)
                with sp.Fori(1, B) as b:
                    chunk_traffic(g * B + b)
            with sp.Fori((G - 1) * B, G * B - 2) as f:
                chunk_traffic(f)
            chunk_traffic(CHUNKS - 2, codes_left=False)
            park(CHUNKS - 1)
            for n, (lo_, hi_) in enumerate(NORM_RANGES[3:]):
                if hi_ <= TT - 4:
                    sp.wait_ge(out_normed, hi_ // 2)
                    sp.wait_ge(out_normed_too, hi_ // 2)
                else:
                    sp.wait_ge(last_normed, hi_ - (TT - 4))
                sp.dma_start(out.rearrange("(t p) d -> p t d", p=P)[:, lo_:hi_, :],
                             acc[:, lo_:hi_, :]).then_inc(out_stored, 16)
            sp.wait_ge(out_stored, 16 * len(NORM_RANGES[3:]))

        @block.gpsimd
        def _(pool):
            def step(front, b, back, back_b, back_g, w_next=None, first_of=None, last=False, ending=False):
                if back is not None:
                    pool.wait_ge(merged, back * 3 + 3)
                    pool.wait_ge(absmax_loaded, back * 32 + 32)
                    nc.gpsimd.tensor_tensor(w_scaled, w_value, absmax_sb[:, :], ALU.mult)
                    nc.gpsimd.tensor_tensor(w_split[:, HI, :].bitcast(F32R), w_value, absmax_sb[:, :],
                                            ALU.mult).then_inc(absmax_used, 1)
                    pool.wait_ge(absmax_used, back + 1)
                    nc.gpsimd.tensor_tensor(w_split[:, LO, :].bitcast(F32R), w_scaled, w_split[:, HI, :],
                                            ALU.subtract).then_inc(w_split_ready, 1)
                if front is not None:
                    for c in range(2):
                        pool.wait_ge(inv_ready, front * 2 + c + 1)
                        tiles = probs[:, c, :].rearrange("p (j m) -> p j m", j=NB)
                        nc.gpsimd.tensor_tensor(tiles, tiles, row_inv[:, c, :].unsqueeze(2).to_broadcast([P, NB, P]),
                                                ALU.mult).then_inc(probs_ready, 1)
                if first_of is not None and back is not None:
                    pool.wait_ge(ones_set, 1)
                    pool.wait_ge(wo_loaded, first_of * 16 + 16)
                    pool.wait_ge(y_done, back * 2 + 2)
                    split_wo(first_of)

            def split_wo(g):
                hi, lo = (wo_parts[:, s, :, :].rearrange("p h d -> p (h d)") for s in (HI, LO))
                nc.gpsimd.tensor_tensor(hi, wo_raw, ones[:, 0:1].to_broadcast([P, HQ * D]), ALU.mult).then_inc(wo_hi, 1)
                pool.wait_ge(wo_hi, g + 1)
                nc.gpsimd.tensor_tensor(lo, wo_raw, f32(hi), ALU.subtract).then_inc(wo_lo, 1)

            pool.wait_ge(ones_set, 1)
            pool.wait_ge(wo_loaded, 16)
            split_wo(0)
            for b in range(LATE, B):
                pool.wait_ge(x_loaded[b], 16)
                nc.gpsimd.tensor_tensor(x_parts[:, HI, :, b * N:(b + 1) * N], x_raw[:, b, :, :],
                                        ones[:, 0:1].unsqueeze(2).to_broadcast([P, KT, N]), ALU.mult).then_inc(x_late_hi, 1)
            step(0, 0, None, None, None, first_of=0)
            for b in range(LATE, B):
                pool.wait_ge(x_late_hi, B - LATE)
                pool.wait_ge(x_lo, b - 1)
                nc.gpsimd.tensor_tensor(x_parts[:, LO, :, b * N:(b + 1) * N], x_raw[:, b, :, :],
                                        f32(x_parts[:, HI, :, b * N:(b + 1) * N]), ALU.subtract).then_inc(x_lo, 1)
            attention_steps(pool, step)
            for n in range(3, 3 + TB - 1):
                lo_, hi_ = NORM_RANGES[n]
                pool.wait_ge(rstd_done, n + 1)
                for t in range(lo_ + 2, hi_):
                    nc.gpsimd.tensor_scalar(acc[:, t, :], acc[:, t, :], mean_var[:, t, 0:1], rstd[:, t:t + 1],
                                            ALU.subtract, ALU.mult).then_inc(out_normed_too, 1)

        @block.tensor
        def _(pe):
            def project(dst, unit, col, b, last_sem, by_halves=False):
                for k in range(KT):
                    if by_halves and k % HALF == 0:
                        pe.wait_ge(x0_lo, k // HALF + 1)
                        pe.wait_ge(w_lo if k else w_half_lo, 1)
                    for n, (s, m) in enumerate(PASSES):
                        mm = nc.tensor.matmul(dst, w_parts[:, s, unit, k, col:col + P],
                                              x_parts[:, m, k, bass.ds(b * N, N)],
                                              start=(k == 0 and n == 0), stop=(k == KT - 1 and n == 2))
                if last_sem is not None:
                    mm.then_inc(last_sem, 1)

            def step(front, b, back, back_b, back_g, w_next=None, first_of=None, last=False, ending=False):
                if front is not None:
                    for c in range(2):
                        if first_of is not None and (back is not None or c > 0):
                            pe.wait_ge(w_lo, first_of * 3 + c + 1)
                        if back is not None:
                            pe.wait_ge(k_lo if c == 0 else v_lo, front)
                        if first_of is None and c == 0:
                            pe.wait_ge(x_lo, b)
                        for h in range(2):
                            project(PROJ[c][:, h * N:(h + 1) * N], c, h * P, b, q_done if h else None,
                                    by_halves=back is None and c == 0 and h == 0)
                if front is None:
                    for t in range(3):
                        turn_x1(t)
                if back is not None:
                    for c in range(2):
                        pe.wait_ge(probs_ready, back * 2 + c + 1)
                    for bp in range(2):
                        for j in (2 * bp, 2 * bp + 1):
                            for c in range(2):
                                at_ = (j % 2) * 256 + c * P
                                mm = nc.tensor.transpose(TURN[bp][:, at_:at_ + P],
                                                         probs[:, c, j * P:(j + 1) * P], ident[:, :])
                        mm.then_inc(probs_turned, 1)
                if front is None:
                    turn_x1(3)
                if front is not None:
                    if first_of is not None:
                        pe.wait_ge(w_lo, first_of * 3 + 3)
                    pe.wait_ge(q_lo, front * 2 + 1)
                    for h in range(2):
                        project(PROJ[0][:, h * N:(h + 1) * N], 2, h * P, b, kv_done if h else None)
                if back is not None:
                    for bp in range(2):
                        pe.wait_ge(pt_lo, back * 2 + bp + 1)
                        pe.wait_ge(y_added, back * 2 + 1 + bp)
                        if bp == 0:
                            runs = ((0, 512, WINDOW[0]),)
                        else:
                            runs = ((0, 256, WINDOW[2]), (256, 512, WINDOW[3]))
                        for lo_, hi_, w in runs:
                            for n, (s, m) in enumerate(PASSES):
                                mm = nc.tensor.matmul(CTX[bp][:, lo_:hi_], v_parts[:, s, w, :],
                                                      pt_parts[:, m, bp, lo_:hi_],
                                                      start=(n == 0), stop=(n == 2))
                        mm.then_inc(ctx_done, 1)
                if front is not None:
                    pe.wait_ge(vT_copied, front + 1)
                    pe.wait_ge(q_lo, front * 2 + 2)
                    if back is None:
                        pe.wait_ge(consts_loaded, 32)
                    for w in range(3):
                        mm = nc.tensor.transpose(PROJ[1][:, w * P:(w + 1) * P],
                                                 vT[:, w * QB:w * QB + P], ident[:, :])
                    mm.then_inc(v_turned, 1)
                    pe.wait_ge(k_lo, front + 1)
                    for c in range(2):
                        for j in range(NB):
                            ws = WINDOW_START[j]
                            nc.tensor.matmul(score[:, c, j, :, :], q_parts[:, HI, c, j, :],
                                             k_parts[:, :, ws:ws + P], start=True, stop=False)
                            mm = nc.tensor.matmul(score[:, c, j, 0, :], q_parts[:, LO, c, j, :],
                                                  k_parts[:, HI, ws:ws + P], start=False, stop=True)
                        mm.then_inc(scores_done, 1)
                if back is not None:
                    pe.wait_ge(wo_lo, back_g + 1)
                    for tt in range(2):
                        pe.wait_ge(o_lo, back * 2 + tt + 1)
                        for h in range(HQ):
                            for n, (s, m) in enumerate(PASSES):
                                mm = nc.tensor.matmul(CTX[tt][:, 0:D], o_parts[:, s, h, tt * P:(tt + 1) * P],
                                                      wo_parts[:, m, h, :], start=(h == 0 and n == 0),
                                                      stop=(h == HQ - 1 and n == 2))
                        mm.then_inc(y_done, 1)

            def turn_x1(t):
                pe.wait_ge(x1_normed, t + 1)
                if t in (6, 7):
                    pe.wait_ge(y_added, 2 * G * B + 2)
                if t >= 8:
                    pe.wait_ge(x1_lo, t - 3)
                for k in range(KT):
                    mm = nc.tensor.transpose(x1_bank(t)[:, k * P:(k + 1) * P],
                                             acc[:, t, k * P:(k + 1) * P], ident[:, :])
                mm.then_inc(x1_turned, 1)

            step(0, 0, None, None, None, first_of=0)
            attention_steps(pe, step)

            GU, DOWN = bank[0:4], bank[4:8]

            def ffn(front, back):
                if front is not None:
                    s, mg, half, tb, wbuf, hbuf = front
                    if tb == 0:
                        pe.wait_ge(ffn_loaded[wbuf], (half + 1) * 16)
                    pe.wait_ge(x1_lo, 4 * (tb + 1))
                    for c in range(2):
                        if back is not None:
                            pe.wait_ge(hid_ready, (s - 1) * 2 + c + 1)
                        for kind in range(2):
                            for k in range(KT):
                                i = kind * 2 + k // 2
                                col = (k % 2) * 256 + c * P
                                for n, (st, mv) in enumerate(PASSES):
                                    mm = nc.tensor.matmul(GU[2 * c + kind],
                                                          ffn_w[wbuf][:, st, i, col:col + P],
                                                          x_parts[:, mv, k, tb * 512:(tb + 1) * 512],
                                                          start=(k == 0 and n == 0),
                                                          stop=(k == KT - 1 and n == 2))
                            if kind == 1:
                                mm.then_inc(gu_done, 1)
                            if back is None:
                                for t in tiles_turned(c, kind):
                                    turn_x1(t)
                if back is not None:
                    s, mg, half, tb, wbuf, hbuf = back
                    if tb == 0:
                        pe.wait_ge(x1_lo, TT)
                    pe.wait_ge(hid_lo, s * 2 + 2)
                    for tt in range(4):
                        pe.wait_ge(y_added, s * 4 + (2 * G * B - 1) + tt)
                        for c in range(2):
                            for n, (st, mv) in enumerate(PASSES):
                                mm = nc.tensor.matmul(DOWN[tt], hid[hbuf][:, st, c, tt * P:(tt + 1) * P],
                                                      ffn_w[wbuf][:, mv, 4 + c, :],
                                                      start=(c == 0 and n == 0), stop=(c == 1 and n == 2))
                        mm.then_inc(down_done, 1)

            ffn_steps(pe, ffn)

        @block.scalar
        def _(act):
            def copy(dst, src):
                return nc.scalar.activation(dst, src, ACT.Copy)

            def load_ffn(mg, wbuf):
                act.dma_start(f32(ffn_w[wbuf]).rearrange("p s i c -> p s (i c)"),
                              parked[:, :, bass.ds(mg * GC, GC)]).then_inc(ffn_loaded[wbuf], 16)

            def step(front, b, back, back_b, back_g, w_next=None, first_of=None, last=False, ending=False):
                if front is not None:
                    for c in range(2):
                        act.wait_ge(q_done, front * 2 + c + 1)
                        copy(q_parts[:, HI, c, :, :].rearrange("p j (h q) -> p j h q", h=2),
                             PROJ[c][:, :].rearrange("p (h j q) -> p j h q", h=2, j=NB)).then_inc(q_hi, 1)
                if front is None:
                    for t in (0, 1):
                        split_x1(t)
                elif back is None:
                    for b_ in range(2, EARLY):
                        round_x(b_)
                if back is not None:
                    for bp in range(2):
                        act.wait_ge(probs_turned, back * 2 + bp + 1)
                        copy(pt_parts[:, HI, bp, :], TURN[bp]).then_inc(pt_hi, 1)
                if ending:
                    std(0)
                if front is None:
                    split_x1(2)
                if front is not None:
                    act.wait_ge(kv_done, front + 1)
                    copy(vT[:, :], PROJ[0][:, N:2 * N]).then_inc(vT_copied, 1)
                    copy(k_parts[:, HI, :], PROJ[0][:, 0:N]).then_inc(k_hi, 1)
                    if ending:
                        assert 2 * GC <= at[1]
                        act.wait_ge(kv_done, G * B)
                        act.wait_ge(parked_sem, 16 * -(-GC // CW))
                        load_ffn(0, 0)
                if back is not None:
                    for bp in range(2):
                        act.wait_ge(ctx_done, back * 2 + bp + 1)
                        copy(o_parts[:, HI, :, bp * P:(bp + 1) * P].rearrange("p h (k q) -> p k h q", k=2),
                             CTX[bp][:, :].rearrange("p (k h q) -> p k h q", k=2, h=HQ)).then_inc(o_hi, 1)
                if front is not None:
                    act.wait_ge(v_turned, front + 1)
                    copy(v_parts[:, HI, :, :].rearrange("p w d -> p (w d)"), PROJ[1][:, 0:3 * P]).then_inc(v_hi, 1)
                    if back is None:
                        for b_ in range(EARLY, LATE):
                            round_x(b_)
                    if w_next is not None:
                        act.wait_ge(kv_done, front + 1)
                        split_w(w_next)
                    for c in range(2):
                        act.wait_ge(neg_max_ready, front * 2 + c + 1)
                        for j in range(NB):
                            at_ = probs[:, c, j * P:(j + 1) * P]
                            e = nc.scalar.activation(at_, at_, ACT.Exp, bias=neg_max[:, c, j:j + 1], scale=SCALE,
                                                     accum_out=row_sum[:, c, j:j + 1])
                        e.then_inc(exp_done, 1)
                    if not ending:
                        pair_values(front)
                if front is None:
                    split_x1(3)
                    std(1)
                    pair_values(CHUNKS - 1)

            def pair_values(f):
                act.wait_ge(bits_ready, f + 1)
                if not isinstance(f, int) or f > 0:
                    act.wait_ge(parked_sem, f * 16)
                for k, (base, slope) in enumerate(code_lines()):
                    pair = nc.scalar.activation(pair_value[:, k, :], code_bits[:, 0, :], ACT.Copy,
                                                bias=base, scale=slope)
                pair.then_inc(pairs_ready, 1)

            def std(n):
                lo_, hi_ = NORM_RANGES[n]
                act.wait_ge(var_done, n + 1)
                if n == 0:
                    act.wait_ge(eps_set, 1)
                nc.scalar.activation(rstd[:, lo_:hi_], mean_var[:, lo_:hi_, 1:2].rearrange("p t a -> p (t a)"),
                                     ACT.Sqrt, bias=eps_sb[:, 0:1]).then_inc(std_done, 1)

            def split_x1(t):
                act.wait_ge(x1_turned, t + 1)
                copy(x_parts[:, HI, :, t * P:(t + 1) * P],
                     x1_bank(t).rearrange("p (k t) -> p k t", k=KT)).then_inc(x1_hi, 1)

            def round_x(b):
                act.wait_ge(x_loaded[b], 16)
                at_ = slice(b * N, (b + 1) * N)
                copy(x_parts[:, HI, :, at_], x_raw[:, b, :, :]).then_inc(x_hi, 1)

            def split_w(g, first_unit=0):
                for u in range(first_unit, 3):
                    act.wait_ge(w_loaded[u], g * 16 + 16)
                    copy(w_parts[:, HI, u, :, :], w_raw[:, u, :].rearrange("p (k c) -> p k c", k=KT)).then_inc(w_hi, 1)

            for half in range(2):
                ks = slice(half * HALF, half * HALF + HALF)
                act.wait_ge(x_loaded[0] if half else x_half_loaded, 16)
                copy(x_parts[:, HI, ks, 0:N], x_raw[:, 0, ks, :]).then_inc(x0_hi, 1)
                act.wait_ge(w_loaded[0] if half else w_half_loaded, 16)
                copy(w_parts[:, HI, 0, ks, :],
                     w_raw[:, 0, half * UW // 2:(half + 1) * UW // 2].rearrange("p (k c) -> p k c", k=HALF)
                     ).then_inc(w_hi if half else w_half_hi, 1)
            split_w(0, 1)
            step(0, 0, None, None, None, first_of=0)
            attention_steps(act, step)

            def ffn(front, back):
                if front is not None:
                    s, mg, half, tb, wbuf, hbuf = front
                    if tb == 1 and not (isinstance(mg, int) and mg == MG - 1):
                        act.wait_ge(gu_done, s * 2 + 1)
                        act.wait_ge(parked_sem, 16 * CHUNKS)
                        load_ffn(mg + 1, 1 - wbuf)
                    for c in range(2):
                        if back is None:
                            for t in tiles_turned(c, 0):
                                split_x1(t)
                        if back is None and c == 0:
                            for n, t in enumerate(tiles_turned(c, 1)):
                                split_x1(t)
                                if n == 1:
                                    std(2)
                        act.wait_ge(gu_done, s * 2 + c + 1)
                        if back is not None:
                            act.wait_ge(hid_ready, (s - 1) * 2 + c + 1)
                        nc.scalar.activation(silu_g[:, c, :], bank[2 * c], ACT.Silu).then_inc(silu_done, 1)
                    for c in range(2):
                        act.wait_ge(hid_ready, s * 2 + c + 1)
                        copy(hid[hbuf][:, HI, c, :], hid_f[:, c, :]).then_inc(hid_hi, 1)
                if back is not None and isinstance(back[1], int) and back[1] == MG - 1:
                    tb = back[3]
                    std(3 + tb)
                    if tb == TB - 1:
                        std(4 + tb)

            ffn_steps(act, ffn)

        @block.vector
        def _(dve):
            def low(dst, src, hi):
                return nc.vector.tensor_tensor(dst, src, f32(hi), ALU.subtract)

            def merge(level):
                view = pair_value[:, :, :].rearrange("p (j a) c -> p j a c", a=1 << level)
                nc.vector.copy_predicated(view[:, :, 0, :], bit_mask(level, 8 >> level),
                                          view[:, :, 1 << (level - 1), :]).then_inc(merged, 1)

            def bit_mask(bit, times):
                return code_bits[:, bit:bit + 1, :].broadcast_to([P, times, CW])

            def take_bits(f):
                codes_u8 = code_sb[:, :].bitcast(mybir.dt.uint8).rearrange("p (c e) -> p c e", e=4)[:, :, 0]
                if not isinstance(f, int) or f > 0:
                    dve.wait_ge(merged, f * 3)
                dve.wait_ge(codes_loaded, f * 16 + 16)
                for bit in range(4):
                    i = nc.vector.tensor_scalar(code_bits[:, bit, :], codes_u8, 1 << bit, None, ALU.bitwise_and)
                i.then_inc(bits_ready, 1)

            def step(front, b, back, back_b, back_g, w_next=None, first_of=None, last=False, ending=False):
                if ending:
                    variances(0)
                if front is None:
                    split_x1(0)
                if front is not None:
                    for c in range(2):
                        dve.wait_ge(q_hi, front * 2 + c + 1)
                        if back is not None and c == 0:
                            dve.wait_ge(pairs_ready, front)
                        low(q_parts[:, LO, c, :, :].rearrange("p j (h q) -> p j h q", h=2),
                            PROJ[c][:, :].rearrange("p (h j q) -> p j h q", h=2, j=NB),
                            q_parts[:, HI, c, :, :].rearrange("p j (h q) -> p j h q", h=2)).then_inc(q_lo, 1)
                        if back is not None and c == 0:
                            merge(1)
                    if back is None:
                        for b_ in range(1, EARLY):
                            split_x(b_)
                if back is not None:
                    for bp in range(2):
                        dve.wait_ge(pt_hi, back * 2 + bp + 1)
                        if front is not None and bp == 0:
                            dve.wait_ge(merged, back * 3 + 1)
                        low(pt_parts[:, LO, bp, :], TURN[bp], pt_parts[:, HI, bp, :]).then_inc(pt_lo, 1)
                    if front is not None:
                        merge(2)
                if front is None:
                    split_x1(1)
                if front is not None:
                    dve.wait_ge(k_hi, front + 1)
                    if back is not None:
                        dve.wait_ge(merged, back * 3 + 2)
                    low(k_parts[:, LO, :], PROJ[0][:, 0:N], k_parts[:, HI, :]).then_inc(k_lo, 1)
                    if back is not None:
                        merge(3)
                if back is not None:
                    for bp in range(2):
                        dve.wait_ge(o_hi, back * 2 + bp + 1)
                        o_view = [o_parts[:, s, :, bp * P:(bp + 1) * P].rearrange("p h (k q) -> p k h q", k=2)
                                  for s in (HI, LO)]
                        low(o_view[LO], CTX[bp][:, :].rearrange("p (k h q) -> p k h q", k=2, h=HQ),
                            o_view[HI]).then_inc(o_lo, 1)
                if front is not None:
                    dve.wait_ge(v_hi, front + 1)
                    low(v_parts[:, LO, :, :].rearrange("p w d -> p (w d)"), PROJ[1][:, 0:3 * P],
                        v_parts[:, HI, :, :].rearrange("p w d -> p (w d)")).then_inc(v_lo, 1)
                    for c in range(2):
                        dve.wait_ge(scores_done, front * 2 + c + 1)
                        if back is None:
                            dve.wait_ge(consts_loaded, 32)
                        nc.vector.tensor_tensor(probs[:, c, :].rearrange("p (j m) -> p j m", j=NB), score[:, c, :, 1, :],
                                                mask_sb[:, :, :], ALU.add).then_inc(masked, 1)
                        dve.wait_ge(consts_loaded, 32)
                        dve.wait_ge(masked, front * 2 + c + 1)
                        for j in range(NB):
                            tile = probs[:, c, j * P:(j + 1) * P]
                            m = nc.vector.tensor_tensor_reduce(
                                out=tile, in0=score[:, c, j, 0, :], in1=tile, scale=1.0, scalar=-3.4e38,
                                op0=ALU.add, op1=ALU.max, accum_out=row_max[:, c, j:j + 1])
                        m.then_inc(max_found, 1)
                        dve.wait_ge(max_found, front * 2 + c + 1)
                        nc.vector.tensor_scalar(neg_max[:, c, :], row_max[:, c, :], -SCALE, None,
                                                ALU.mult).then_inc(neg_max_ready, 1)
                    if w_next is not None:
                        split_w(w_next, 0)
                    for c in range(2):
                        dve.wait_ge(exp_done, front * 2 + c + 1)
                        nc.vector.reciprocal(row_inv[:, c, :], row_sum[:, c, :]).then_inc(inv_ready, 1)
                        if c == 0 and w_next is None and not ending:
                            take_bits(front)
                        if c == 0 and ending:
                            invert_std(0)
                            for t in range(3):
                                norm(t).then_inc(x1_normed, 1)
                    if w_next is not None:
                        take_bits(front)
                        split_w(w_next, 1)
                        split_w(w_next, 2)
                    if back is None:
                        for b_ in range(EARLY, LATE):
                            split_x(b_)
                if front is None:
                    sequence_stats(B - 2)
                    for t in (2, 3):
                        split_x1(t)
                    variances(1)
                    take_bits(CHUNKS - 1)
                    invert_std(1)
                    for t in range(4, 8):
                        norm(t).then_inc(x1_normed, 1)
                if back is not None:
                    for tt in range(2):
                        dve.wait_ge(y_done, back * 2 + tt + 1)
                        dve.wait_ge(acc_loaded, 32)
                        row = acc[:, bass.ds(back_b * 2 + tt, 1), :].rearrange("p a d -> p (a d)")
                        nc.vector.tensor_tensor(row, CTX[tt][:, :], row, ALU.add).then_inc(y_added, 1)
                    if last:
                        dve.wait_ge(y_added, back * 2 + 4)
                        if ending:
                            norm(3).then_inc(x1_normed, 1)
                        elif front is not None:
                            sequence_stats(back_b)
                if front is None:
                    for t in range(8, 12):
                        norm(t).then_inc(x1_normed, 1)

            def sequence_stats(b):
                for tt in range(2):
                    i = nc.vector.bn_stats(stats[:, bass.ds(b * 2 + tt, 1), :].rearrange("p a s -> p (a s)"),
                                           acc[:, bass.ds(b * 2 + tt, 1), :].rearrange("p a d -> p (a d)"))
                i.then_inc(stats_done, 1)

            def split_w(g, u):
                dve.wait_ge(w_hi, g * 3 + u + 1)
                low(w_parts[:, LO, u, :, :], w_raw[:, u, :].rearrange("p (k c) -> p k c", k=KT),
                    w_parts[:, HI, u, :, :]).then_inc(w_lo, 1)

            def split_x(b):
                at_ = slice(b * N, (b + 1) * N)
                if b == 1:
                    dve.wait_ge(x_loaded[b], 16)
                    nc.vector.tensor_copy(x_parts[:, HI, :, at_], x_raw[:, b, :, :]).then_inc(x1st_hi, 1)
                    dve.wait_ge(x1st_hi, 1)
                else:
                    dve.wait_ge(x_hi, b - 1)
                low(x_parts[:, LO, :, at_], x_raw[:, b, :, :], x_parts[:, HI, :, at_]).then_inc(x_lo, 1)

            def variances(n):
                lo_, hi_ = NORM_RANGES[n]
                dve.wait_ge(stats_done, hi_ // 2 if n < 3 else B + hi_)
                for t in range(lo_, hi_):
                    i = nc.vector.bn_aggr(mean_var[:, t, :], stats[:, t, :])
                i.then_inc(var_done, 1)

            def invert_std(n):
                lo_, hi_ = NORM_RANGES[n]
                dve.wait_ge(std_done, n + 1)
                nc.vector.reciprocal(rstd[:, lo_:hi_], rstd[:, lo_:hi_]).then_inc(rstd_done, 1)
                dve.wait_ge(rstd_done, n + 1)

            def norm(t):
                return nc.vector.tensor_scalar(acc[:, t, :], acc[:, t, :], mean_var[:, t, 0:1], rstd[:, t:t + 1],
                                               ALU.subtract, ALU.mult)

            def split_x1(t):
                dve.wait_ge(x1_hi, t + 1)
                low(x_parts[:, LO, :, t * P:(t + 1) * P], x1_bank(t).rearrange("p (k t) -> p k t", k=KT),
                    x_parts[:, HI, :, t * P:(t + 1) * P]).then_inc(x1_lo, 1)

            nc.vector.memset(eps_sb[:, :], LN_EPS).then_inc(eps_set, 1)
            nc.vector.memset(row_max[:, :, :], 0.0).then_inc(y_added, 2)
            nc.vector.memset(ones[:, :], 1.0).then_inc(ones_set, 1)
            for half in range(2):
                ks = slice(half * HALF, half * HALF + HALF)
                dve.wait_ge(x0_hi, half + 1)
                low(x_parts[:, LO, ks, 0:N], x_raw[:, 0, ks, :], x_parts[:, HI, ks, 0:N]).then_inc(x0_lo, 1)
                dve.wait_ge(w_hi if half else w_half_hi, 1)
                low(w_parts[:, LO, 0, ks, :],
                    w_raw[:, 0, half * UW // 2:(half + 1) * UW // 2].rearrange("p (k c) -> p k c", k=HALF),
                    w_parts[:, HI, 0, ks, :]).then_inc(w_lo if half else w_half_lo, 1)
            for u in range(1, 3):
                split_w(0, u)
            step(0, 0, None, None, None, first_of=0)
            attention_steps(dve, step)

            def ffn(front, back):
                if front is not None:
                    s, mg, half, tb, wbuf, hbuf = front
                    for c in range(2):
                        if back is None:
                            for t in tiles_turned(c, 0):
                                split_x1(t)
                        if back is None and c == 0:
                            sequence_stats(B - 1)
                            variances(2)
                            for t in range(12, TT - 2):
                                norm(t).then_inc(x1_normed, 1)
                            invert_std(2)
                            for t in range(TT - 2, TT):
                                norm(t).then_inc(x1_normed, 1)
                            for t in tiles_turned(c, 1):
                                split_x1(t)
                        dve.wait_ge(silu_done, s * 2 + c + 1)
                        if back is not None:
                            dve.wait_ge(hid_lo, (s - 1) * 2 + c + 1)
                        nc.vector.tensor_tensor(hid_f[:, c, :], bank[2 * c + 1], silu_g[:, c, :],
                                                ALU.mult).then_inc(hid_ready, 1)
                        if back is None and c == 0:
                            dve.wait_ge(pairs_ready, CHUNKS)
                            for level in range(1, 4):
                                merge(level)
                                if level < 3:
                                    dve.wait_ge(merged, (CHUNKS - 1) * 3 + level)
                    for c in range(2):
                        dve.wait_ge(hid_hi, s * 2 + c + 1)
                        low(hid[hbuf][:, LO, c, :], hid_f[:, c, :], hid[hbuf][:, HI, c, :]).then_inc(hid_lo, 1)
                if back is not None:
                    s, mg, half, tb, wbuf, hbuf = back
                    final = isinstance(mg, int) and mg == MG - 1
                    for tt in range(4):
                        dve.wait_ge(down_done, s * 4 + tt + 1)
                        row = acc[:, tb * 4 + tt, :]
                        nc.vector.tensor_tensor(row, bank[4 + tt], row, ALU.add).then_inc(y_added, 1)
                        if final and tt > 0:
                            tile_stats(s, tb, tt - 1)
                        if final and tb == TB - 1 and tt == 2:
                            variances(3 + tb)
                        if final and tb == TB - 1 and tt == 3:
                            last_norm(3 + tb)
                    if final:
                        tile_stats(s, tb, 3)
                        if tb < TB - 1:
                            variances(3 + tb)
                            invert_std(3 + tb)
                            for t in (4 * tb, 4 * tb + 1):
                                norm(t).then_inc(out_normed, 1)
                        else:
                            variances(4 + tb)
                            last_norm(4 + tb)

            def tile_stats(s, tb, tt):
                dve.wait_ge(y_added, 2 * G * B + 2 + 4 * s + tt + 1)
                nc.vector.bn_stats(stats[:, 4 * tb + tt, :], acc[:, 4 * tb + tt, :]).then_inc(stats_done, 1)

            def last_norm(n):
                invert_std(n)
                for t in range(*NORM_RANGES[n]):
                    norm(t).then_inc(last_normed, 1)

            ffn_steps(dve, ffn)


def kernel(L0_attn_x, L0_attn_wq, L0_attn_wk, L0_attn_wv, L0_attn_wo, L0_ffn_gate_q, L0_ffn_gate_absmax,
           L0_ffn_up_q, L0_ffn_up_absmax, L0_ffn_down_q, L0_ffn_down_absmax):
    import concourse.bacc as bacc
    from concourse.bass_utils import run_bass_kernel_spmd

    x, wq, wk, wv, wo = (np.asarray(a) for a in (L0_attn_x, L0_attn_wq, L0_attn_wk, L0_attn_wv, L0_attn_wo))
    B, N, D = x.shape
    T, KT, G = B * N, D // P, wk.shape[0] // P
    HQ = wq.shape[0] // P // G
    M = np.asarray(L0_ffn_gate_q).shape[0]
    MG = M // 256

    tokens = x.reshape(T, D)
    xT = tokens.T.reshape(KT, P, T).transpose(1, 0, 2)
    heads = np.concatenate([wq.reshape(G, HQ, P, D), wk.reshape(G, 1, P, D), wv.reshape(G, 1, P, D)], axis=1)
    w_qkv = heads.reshape(G, 3, 256, KT, P).transpose(0, 4, 1, 3, 2).reshape(G, P, -1)
    w_o = wo.reshape(D, G, HQ, P).transpose(1, 3, 2, 0).reshape(G, P, -1)

    def up_chunks(q, absmax):
        q = np.asarray(q).reshape(MG, 256, 2, 2, P).transpose(0, 2, 4, 3, 1).reshape(MG, 2, P, 512)
        a = np.asarray(absmax).reshape(MG, 256, 2, 2, 2).transpose(0, 2, 4, 3, 1).reshape(MG, 2, 2, 512)
        return q, a

    def down_chunks(q, absmax):
        q = np.asarray(q).reshape(D, MG, 2, P).transpose(1, 2, 3, 0)
        a = np.asarray(absmax).reshape(D, MG, 2, 2).transpose(1, 2, 3, 0)
        return q, a

    parts = [up_chunks(L0_ffn_gate_q, L0_ffn_gate_absmax), up_chunks(L0_ffn_up_q, L0_ffn_up_absmax),
             down_chunks(L0_ffn_down_q, L0_ffn_down_absmax)]
    codes, absmax = (np.concatenate([p[n] for p in parts], axis=1) for n in range(2))
    codes = codes.transpose(2, 0, 1, 3).reshape(P, G * B, -1).transpose(1, 0, 2)
    absmax = absmax.transpose(2, 0, 1, 3).reshape(2, G * B, -1).transpose(1, 0, 2)

    i, m = np.arange(P)[:, None] % 64, np.arange(P)[None, :]
    first = np.where(m <= i, 0.0, MASKED)
    later = np.where((m > i) & (m <= i + 64), 0.0, MASKED)
    masks = np.stack([first, later, later, later], axis=1).astype(np.float32)

    nc = bacc.Bacc("TRN2", target_bir_lowering=False, num_devices=1)
    arrays, ins = {}, []
    for name, a in (("x", tokens), ("xT", xT), ("w_qkv", w_qkv), ("w_o", w_o), ("codes", codes),
                    ("absmax", absmax), ("masks", masks), ("identity", np.eye(P, dtype=np.float32))):
        a = np.ascontiguousarray(a)
        arrays[name] = a
        ins.append(nc.dram_tensor(name, a.shape, mybir.dt.from_np(a.dtype), kind="ExternalInput").ap())
    out = nc.dram_tensor("out", (T, D), F32, kind="ExternalOutput").ap()
    decoder_layer(nc, *ins, out)
    r = run_bass_kernel_spmd(nc, [arrays], core_ids=[0])
    return np.asarray(r.results[0]["out"]).reshape(B, N, D)
```
